# Optimizing a Trainium2 kernel written in Bass

```python
import numpy as np
import jax
import jax.numpy as jnp

def _softmax(x, axis=-1):
    return jax.nn.softmax(x, axis=axis)

def _gelu(x):
    return jax.nn.gelu(x, approximate=True)

def _silu(x):
    return jax.nn.silu(x)

def _sigmoid(x):
    return jax.nn.sigmoid(x)

def _layernorm(x, axis=-1, eps=1e-05):
    m = jnp.mean(x, axis=axis, keepdims=True)
    v = jnp.var(x, axis=axis, keepdims=True)
    return (x - m) / jnp.sqrt(v + eps)

def _scatter_add(tgt, idx, src, axis=0):
    return tgt.at[idx].add(src)

def _segment_sum(src, seg, n):
    return jax.ops.segment_sum(src, seg, n)
kernel_name = 'mk_hybrid_d1_jaxref_r8_8713a9'

def setup_inputs(seed: int=0):
    np.random.seed(seed)
    _w = jnp.asarray

    def _L0_attn_a_setup():
        import jax, jax.numpy as jnp
        import numpy as np
        import math
        B, L, D, H = (2, 256, 128, 16)

        def _log_sparse_mask(L):
            m = np.zeros((L, L), dtype=bool)
            for i in range(L):
                for k in range(int(math.log2(i + 1)) + 1):
                    j = i - 2 ** k
                    if j >= 0:
                        m[i, j] = True
                m[i, i] = True
            return m
        key = jax.random.key(seed)
        ks = jax.random.split(key, 9)
        s = 0.02
        return {'x': jax.random.normal(ks[0], (B, L, D), dtype=jnp.float32), 'Wq': jax.random.normal(ks[1], (D, D), dtype=jnp.float32) * s, 'bq': jnp.zeros((D,), dtype=jnp.float32), 'Wk': jax.random.normal(ks[2], (D, D), dtype=jnp.float32) * s, 'bk': jnp.zeros((D,), dtype=jnp.float32), 'Wv': jax.random.normal(ks[3], (D, D), dtype=jnp.float32) * s, 'bv': jnp.zeros((D,), dtype=jnp.float32), 'Wo': jax.random.normal(ks[4], (D, D), dtype=jnp.float32) * s, 'bo': jnp.zeros((D,), dtype=jnp.float32)}
    _L0_attn_a_in = _L0_attn_a_setup()

    def _L0_attn_b_setup():
        import jax, jax.numpy as jnp
        import numpy as np
        D_MODEL = 128
        NUM_HEADS = 16
        D_HEAD = 64
        N_CTX = 256
        BATCH = 4
        NEG_INF = -10000000000.0
        key = jax.random.key(seed)
        k1, k2, k3, k4, k5 = jax.random.split(key, 5)
        s = 1.0 / np.sqrt(D_MODEL).astype(np.float32)
        x = jax.random.normal(k1, (BATCH, N_CTX, D_MODEL), dtype=jnp.float32)
        W_K = jax.random.normal(k2, (NUM_HEADS, D_HEAD, D_MODEL), dtype=jnp.float32) * s
        W_Q = jax.random.normal(k3, (NUM_HEADS, D_HEAD, D_MODEL), dtype=jnp.float32) * s
        W_V = jax.random.normal(k4, (NUM_HEADS, D_HEAD, D_MODEL), dtype=jnp.float32) * s
        W_O = jax.random.normal(k5, (D_MODEL, NUM_HEADS * D_HEAD), dtype=jnp.float32) * s
        return {'x': x, 'W_K': W_K, 'W_Q': W_Q, 'W_V': W_V, 'W_O': W_O}
    _L0_attn_b_in = _L0_attn_b_setup()

    def _L0_ffn_setup():
        import jax, jax.numpy as jnp
        import numpy as np
        E, D, F = (8, 128, 512)
        B, S = (4, 256)

        def _layernorm(x, g, b, eps=1e-05):
            mu = jnp.mean(x, axis=-1, keepdims=True)
            var = jnp.var(x, axis=-1, keepdims=True)
            return (x - mu) * jax.lax.rsqrt(var + eps) * g + b
        key = jax.random.key(seed)
        ks = jax.random.split(key, 5)
        return {'input_features': jax.random.normal(ks[0], (B, S, D), jnp.float32), 'centroids': jax.random.normal(ks[1], (E, D), jnp.float32) * 0.1, 'ln_g': jnp.ones((E, D), jnp.float32), 'ln_b': jnp.zeros((E, D), jnp.float32), 'w1': jax.random.normal(ks[2], (E, F, D), jnp.float32) * (1.0 / np.sqrt(D).astype(np.float32)), 'b1': jnp.zeros((E, F), jnp.float32), 'w2': jax.random.normal(ks[3], (E, D, F), jnp.float32) * (1.0 / np.sqrt(F).astype(np.float32)), 'b2': jnp.zeros((E, D), jnp.float32)}
    _L0_ffn_in = _L0_ffn_setup()
    _d = {'L0_attn_a_x': _L0_attn_a_in['x'], 'L0_attn_a_Wq': _L0_attn_a_in['Wq'], 'L0_attn_a_bq': _L0_attn_a_in['bq'], 'L0_attn_a_Wk': _L0_attn_a_in['Wk'], 'L0_attn_a_bk': _L0_attn_a_in['bk'], 'L0_attn_a_Wv': _L0_attn_a_in['Wv'], 'L0_attn_a_bv': _L0_attn_a_in['bv'], 'L0_attn_a_Wo': _L0_attn_a_in['Wo'], 'L0_attn_a_bo': _L0_attn_a_in['bo'], 'L0_attn_b_W_K': _L0_attn_b_in['W_K'], 'L0_attn_b_W_Q': _L0_attn_b_in['W_Q'], 'L0_attn_b_W_V': _L0_attn_b_in['W_V'], 'L0_attn_b_W_O': _L0_attn_b_in['W_O'], 'L0_ffn_centroids': _L0_ffn_in['centroids'], 'L0_ffn_ln_g': _L0_ffn_in['ln_g'], 'L0_ffn_ln_b': _L0_ffn_in['ln_b'], 'L0_ffn_w1': _L0_ffn_in['w1'], 'L0_ffn_b1': _L0_ffn_in['b1'], 'L0_ffn_w2': _L0_ffn_in['w2'], 'L0_ffn_b2': _L0_ffn_in['b2']}
    _x0 = _d['L0_attn_a_x']
    _d['L0_attn_a_x'] = jax.random.normal(jax.random.fold_in(jax.random.key(seed), 1), (8, 256, 128), dtype=_x0.dtype)
    del _x0
    return _d

def reference(L0_attn_a_x, L0_attn_a_Wq, L0_attn_a_bq, L0_attn_a_Wk, L0_attn_a_bk, L0_attn_a_Wv, L0_attn_a_bv, L0_attn_a_Wo, L0_attn_a_bo, L0_attn_b_W_K, L0_attn_b_W_Q, L0_attn_b_W_V, L0_attn_b_W_O, L0_ffn_centroids, L0_ffn_ln_g, L0_ffn_ln_b, L0_ffn_w1, L0_ffn_b1, L0_ffn_w2, L0_ffn_b2):

    def _L0_attn_a_ref(x, Wq, bq, Wk, bk, Wv, bv, Wo, bo):
        import jax, jax.numpy as jnp
        import numpy as np
        import math
        B, L, D, H = (2, 256, 128, 16)

        def _log_sparse_mask(L):
            m = np.zeros((L, L), dtype=bool)
            for i in range(L):
                for k in range(int(math.log2(i + 1)) + 1):
                    j = i - 2 ** k
                    if j >= 0:
                        m[i, j] = True
                m[i, i] = True
            return m
        Bx, Lx, Dx = x.shape
        dh = Dx // H
        scale = math.sqrt(dh)
        mask = jnp.asarray(_log_sparse_mask(Lx))
        q = (x @ Wq.T + bq).reshape(Bx, Lx, H, dh)
        k = (x @ Wk.T + bk).reshape(Bx, Lx, H, dh)
        v = (x @ Wv.T + bv).reshape(Bx, Lx, H, dh)
        raw = jnp.einsum('blhd,bmhd->bhlm', q, k)
        scores = jnp.where(mask, raw, 0.0) / scale
        attn = jax.nn.softmax(scores, axis=-1)
        out = jnp.einsum('bhlm,bmhd->blhd', attn, v).reshape(Bx, Lx, Dx)
        return out @ Wo.T + bo

    def _L0_attn_b_ref(x, W_K, W_Q, W_V, W_O):
        import jax, jax.numpy as jnp
        import numpy as np
        D_MODEL = 128
        NUM_HEADS = 16
        D_HEAD = 64
        N_CTX = 256
        BATCH = 4
        NEG_INF = -10000000000.0
        b, q_len, d_model = x.shape
        d_head = W_K.shape[1]
        K = jnp.einsum('bpd,ihd->biph', x, W_K)
        Q = jnp.einsum('bpd,ihd->biph', x, W_Q)
        V = jnp.einsum('bpd,ihd->biph', x, W_V)
        scores = jnp.einsum('biph,biqh->biqp', K, Q)
        mask = jnp.tril(jnp.ones((q_len, q_len), dtype=bool))
        scores = jnp.where(mask[None, None, :, :], scores, NEG_INF)
        attn = jax.nn.softmax(scores / np.sqrt(d_head).astype(np.float32), axis=-1)
        z = jnp.einsum('biph,biqp->biqh', V, attn)
        z_flat = jnp.transpose(z, (0, 2, 1, 3)).reshape(b, q_len, -1)
        out = jnp.einsum('bqf,df->bqd', z_flat, W_O)
        return out

    def _L0_ffn_ref(input_features, centroids, ln_g, ln_b, w1, b1, w2, b2):
        import jax, jax.numpy as jnp
        import numpy as np
        E, D, F = (8, 128, 512)
        B, S = (4, 256)

        def _layernorm(x, g, b, eps=1e-05):
            mu = jnp.mean(x, axis=-1, keepdims=True)
            var = jnp.var(x, axis=-1, keepdims=True)
            return (x - mu) * jax.lax.rsqrt(var + eps) * g + b
        Bf, Sf, Df = input_features.shape
        x = input_features.reshape(-1, Df)
        aff = x @ centroids.T
        assign = jnp.argmax(aff, axis=1)
        order = jnp.argsort(assign)
        xs = x[order]
        es = assign[order]
        alpha = jax.nn.sigmoid(jnp.take_along_axis(aff[order], es[:, None], axis=1))
        nE = centroids.shape[0]
        y = jnp.zeros_like(xs)
        for e in range(nE):
            h = _layernorm(xs, ln_g[e], ln_b[e])
            h = jax.nn.relu(h @ w1[e].T + b1[e])
            ye = xs + h @ w2[e].T + b2[e]
            y = y + jnp.where((es == e)[:, None], ye, 0.0)
        out_sorted = alpha * y + (1.0 - alpha) * xs
        inv = jnp.argsort(order)
        return out_sorted[inv].reshape(Bf, Sf, Df)
    x = L0_attn_a_x
    x = x + _L0_attn_a_ref(_layernorm(x, axis=-1), L0_attn_a_Wq, L0_attn_a_bq, L0_attn_a_Wk, L0_attn_a_bk, L0_attn_a_Wv, L0_attn_a_bv, L0_attn_a_Wo, L0_attn_a_bo)
    x = x + _L0_ffn_ref(_layernorm(x, axis=-1), L0_ffn_centroids, L0_ffn_ln_g, L0_ffn_ln_b, L0_ffn_w1, L0_ffn_b1, L0_ffn_w2, L0_ffn_b2)
    x = x + _L0_attn_b_ref(_layernorm(x, axis=-1), L0_attn_b_W_K, L0_attn_b_W_Q, L0_attn_b_W_V, L0_attn_b_W_O)
    x = x + _L0_ffn_ref(_layernorm(x, axis=-1), L0_ffn_centroids, L0_ffn_ln_g, L0_ffn_ln_b, L0_ffn_w1, L0_ffn_b1, L0_ffn_w2, L0_ffn_b2)
    return x

_drawn_inputs = setup_inputs


def setup_inputs(seed=0):
    import zlib

    import numpy as np

    out = dict(_drawn_inputs(seed))
    spreads = {'L0_attn_a_bq': (0.0, 0.8),
     'L0_attn_a_bk': (0.0, 0.8),
     'L0_attn_a_bv': (0.0, 0.1),
     'L0_attn_a_bo': (0.0, 0.1),
     'L0_ffn_ln_g': (1.0, 0.2),
     'L0_ffn_ln_b': (0.0, 0.1),
     'L0_ffn_b1': (0.0, 0.1),
     'L0_ffn_b2': (0.0, 0.1)}
    factors = {'L0_attn_a_Wq': 8.0, 'L0_attn_a_Wk': 8.0, 'L0_attn_a_Wv': 2.811}
    for name, (base, spread) in spreads.items():
        noise = np.random.default_rng([zlib.crc32(name.encode()), seed]).standard_normal(out[name].shape)
        drawn = base * np.exp(spread * noise) if base else spread * noise
        out[name] = jnp.asarray(drawn.astype(out[name].dtype))
    for name, factor in factors.items():
        out[name] = (out[name] * factor).astype(out[name].dtype)
    return out
```

```python
from contextlib import ExitStack

import concourse.bass as bass
from concourse import mybir

F32 = mybir.dt.float32
BF16 = mybir.dt.bfloat16
I32 = mybir.dt.int32
ALU = mybir.AluOpType
ACT = mybir.ActivationFunctionType
AX = mybir.AxisListType

P = 128
NB = 8
L = 256
T = L // P
NT = NB * T
D = 128
EPS = 1e-5

HA = 16
DHA = D // HA
DELTAS = [128, 64, 32, 16, 8, 4, 2, 1, 0]
ND = len(DELTAS)
NS = ND + 1
ISCALE_A = float(DHA) ** -0.5
PAIRS = [(s, P - DELTAS[s], DELTAS[s] - DELTAS[s + 1]) for s in range(0, ND - 1, 2)]
DVE_PAIRS, POOL_PAIRS = PAIRS[2:], PAIRS[:2]
GROUPS_A = [(0, 4), (4, NT)]

HB = 16
DHB = 64
NPAIR = HB // 2
RING = 4
BLOCKS = 3
MASKED = -1e30

NE = 8
F = 512
FC = F // P
AHEAD = 4
NSLOT = (NB * L + NE * (P - 1)) // P

C_ID, C_HEAD, C_BEFORE, C_CAUSAL, C_FIRST, C_UPTO, C_SLOT = 0, 128, 144, 272, 400, 408, 472
C_COLS = C_SLOT + NSLOT


def constants():
    import numpy as np
    c = np.zeros((P, C_COLS), np.float32)
    r = np.arange(P)
    c[:, C_ID:C_ID + P] = np.eye(P)
    c[:, C_HEAD:C_HEAD + HA] = r[:, None] // DHA == np.arange(HA)[None]
    c[:, C_BEFORE:C_BEFORE + P] = r[:, None] < r[None]
    c[:, C_CAUSAL:C_CAUSAL + P] = np.where(r[None] > r[:, None], MASKED, 0.0)
    c[:, C_FIRST:C_FIRST + NE] = NE - np.arange(NE)
    e = np.arange(NE)
    c[:, C_UPTO:C_UPTO + NE * NE] = (e[None] <= e[:, None]).astype(np.float32).reshape(-1)
    c[:, C_SLOT:C_SLOT + NSLOT] = np.arange(NSLOT)
    return c


def view(tile, offset, dims, rows=P):
    step = tile[:].ap[0][0]
    return bass.AP(tile, offset, [[step, rows]] + [list(d) for d in dims])


class Own:

    def __init__(self, eng, sem, per):
        self.eng, self.sem, self.per, self.n = eng, sem, per, 0

    def turn(self, b):
        assert self.n in (0, self.per)
        self.base, self.n = b * self.per, 0

    def after(self, ins):
        self.n += 1
        assert self.n <= self.per
        ins.then_inc(self.sem, 1)
        self.eng.wait_ge(self.sem, self.base + self.n)


def need(eng, sem, n):
    if not isinstance(n, int) or n > 0:
        eng.wait_ge(sem, n)


def hybrid_layer(nc, x_in, w_a, wo_a, b_a, bo_a, w_b, wo_b, cent, ln_gb, w1, b1, w2, b2, const, out):
    ctx = ExitStack()
    with ctx:
        def sb(name, shape, dt=F32):
            return ctx.enter_context(nc.sbuf_tensor(name, shape, dt))

        def sem(name):
            return ctx.enter_context(nc.semaphore(name))

        def sems(prefix, names):
            return [sem(prefix + n) for n in names.split()]

        bank = [ctx.enter_context(nc.psum_tensor(f"bank{i}", [P, 512], F32)) for i in range(3)]
        wide = ctx.enter_context(nc.psum_tensor("wide", [P, 5 * 512], F32))

        cst = sb("cst", [P, C_COLS])
        ident = cst[:, C_ID:C_ID + P]
        xres = sb("xres", [P, NT * D])

        wa = sb("wa", [P, 3 * D])
        woa = sb("woa", [P, D])
        ba = sb("ba", [P, 3])
        boa = sb("boa", [1, D])
        ones_row = sb("ones_row", [1, P])
        stat = sb("stat", [P, NT * 6])
        mv = sb("mv", [P, NT * 2])
        veps = sb("veps", [P, NT])
        rstd = sb("rstd", [P, NT])
        mhalf = sb("mhalf", [P, NT])
        xn = sb("xn", [P, T * D])
        xnT = sb("xnT", [P, L])
        qT = sb("qT", [P, L])
        kT = sb("kT", [P, P + L])
        vT = sb("vT", [P, NB * (P + L)])
        vsum = sb("vsum", [P, NB])
        prod = sb("prod", [P, ND * L])
        smax = sb("smax", [P, T * HA])
        ex = sb("ex", [P, T * NS * HA])
        wgt = sb("wgt", [P, T * NS * HA])
        zsum = sb("zsum", [P, T * HA])
        zall = sb("zall", [P, T * HA])
        zinv = sb("zinv", [P, T * HA])
        wide_w = sb("wide_w", [P, T * NS * D])
        pv = sb("pv", [P, ND * L])
        base = sb("base", [P, L])
        sum4 = sb("sum4", [P, 4 * L])
        sum2 = sb("sum2", [P, 2 * L])
        sum1 = sb("sum1", [P, L])
        oT = sb("oT", [P, L])

        gb = sb("gb", [P, 2 * NE])
        cent_s = sb("cent_s", [P, NE])
        w1s = sb("w1s", [P, NE * F])
        w2s = sb("w2s", [P, NE * FC * D])
        b1r = sb("b1r", [1, NE * F])
        b2r = sb("b2r", [1, NE * D])
        bias1 = sb("bias1", [P, NE * F])
        bias2 = sb("bias2", [P, NE * D])
        before = sb("before", [P, P], BF16)
        ones_bf = sb("ones_bf", [P, P], BF16)
        zero = sb("zero", [P, D])
        vhat = sb("vhat", [P, NT * D])
        back = vhat
        var2 = sb("var2", [P, NT])
        veps2 = sb("veps2", [P, NT])
        rstd2 = sb("rstd2", [P, NT])
        amax = sb("amax", [P, NT])
        alpha = sb("alpha", [P, NT])
        pick = sb("pick", [P, NT * NE])
        pick2 = sb("pick2", [P, NT * NE])
        pmax = sb("pmax", [P, NT])
        onehot = sb("onehot", [P, NT * NE], BF16)
        tiles = sb("tiles", [P, NE])
        tiles_r = sb("tiles_r", [P, NE])
        upto = sb("upto", [P, NE * NE])
        end = sb("end", [P, NE])
        start = sb("start", [P, NE])
        start_r = sb("start_r", [P, NE])
        past = sb("past", [P, NSLOT * NE])
        owner_f = sb("owner_f", [P, NSLOT])
        owner = sb("owner", [P, NSLOT], I32)
        row_f = sb("row_f", [P, NT])
        row = sb("row", [P, NT], I32)
        xs = [sb(f"xs{i}", [P, D]) for i in range(AHEAD)]
        xsT = [sb(f"xsT{i}", [P, P]) for i in range(2)]
        hid = sb("hid", [P, F])
        hT = [sb(f"hT{i}", [P, F]) for i in range(2)]
        ys = [sb(f"ys{i}", [P, D]) for i in range(2)]
        xs_dram = nc.dram_tensor("sorted_in", (NSLOT * P, D), F32, kind="Internal").ap()
        ys_dram = nc.dram_tensor("sorted_out", (NSLOT * P, D), F32, kind="Internal").ap()

        wb = sb("wb", [P, 3 * HB * DHB])
        wob = sb("wob", [P, NPAIR * D])
        id_bf = sb("id_bf", [P, P], BF16)
        causal = sb("causal", [P, P], BF16)
        qk = sb("qk", [P, RING * 2 * L])
        vb = sb("vb", [P, T * HB * DHB])
        nmax = sb("nmax", [P, 2 * 2 * T])
        psum = sb("psum", [P, 2 * 2 * T])
        pb = sb("pb", [P, 2 * 2 * BLOCKS * P])
        pT = sb("pT", [P, 2 * BLOCKS * P])
        prec = sb("prec", [P, 2 * T])
        zT = pv

        in_x = [sem(f"in_x{i}") for i in range(4)]
        in_a, zeroed, stored = sems("", "in_a zeroed stored")
        (a_ve, a_rs, a_xn, a_xT, a_xTs, a_proj, a_qkv, a_qk, a_qkp, a_s, a_sm, a_e, a_w, a_ww, a_wT, a_pv, a_sum, a_y,
         a_x) = sems("a_", "ve rs xn xT xTs proj qkv qk qkp s sm e w ww wT pv sum y x")
        in_f, in_b, in_r, filled = sems("", "in_f in_b in_r filled")
        (f_ve, f_rs, f_ve2, f_rs2, f_u, f_uT, f_uTs, f_aff, f_res, f_vh, f_oh, f_am, f_ea, f_rank, f_own,
         f_row, f_bias, f_biass, f_w1, f_sent, f_tx, f_xs, f_h, f_hb, f_th, f_hr, f_y, f_ys, f_x) = sems(
            "f_", "ve rs ve2 rs2 u uT uTs aff res vh oh am ea rank own row bias biass w1 sent tx xs h hb th hr y ys x")
        f_ld, f_st = [sem(f"f_ld{i}") for i in range(AHEAD)], [sem(f"f_st{i}") for i in range(2)]
        f_back = [sem(f"f_back{i}") for i in range(4)]
        (b_w, b_xn, b_xT, b_xTs, b_j, b_qk, b_vp, b_v, b_s, b_mx, b_e, b_n, b_t, b_ta, b_tb, b_pv,
         b_zTs, b_o, b_x) = sems("b_", "w xn xT xTs j qk vp v s mx e n t ta tb pv zTs o x")
        own_ln, own_sm, own_w, own_pv, own_sum, own_f, own_n = sems("own_", "ln sm w pv sum f n")

        block = ctx.enter_context(nc.Block())

        def rolled(eng, ahead, behind, turn):
            for i in range(-ahead, behind):
                turn(i)
            with eng.Fori(behind, NB - ahead) as i:
                turn(i)
            for i in range(NB - ahead, NB + behind):
                turn(i)

        def slot_turns(turn):
            for s in range(NSLOT):
                turn(s, s // 2, s % 2)

        def experts(engine):
            return nc.values_load_multi_w_load_instructions(
                owner[0:1, :], engines=[engine], min_val=0, max_val=(NE - 1) * F)[1]

        def seen(k, s, ring):
            return k * ((NSLOT - 1 - s % ring) // ring + 1) + s // ring

        jb = wide[:, 4 * 512:5 * 512]

        def at(b, p):
            return (b + p // NPAIR, p % NPAIR)

        def g_(g):
            return g[0] * NPAIR + g[1]

        def g_mod(g, n):
            return g[1] % n

        def pair_ok(b, p):
            return not isinstance(b, int) or b * NPAIR + p < NB * NPAIR

        def all_steps(eng, step):
            for p in range(NPAIR):
                step(0, p)
            with eng.Fori(1, NB - 1) as b:
                for p in range(NPAIR):
                    step(b, p)
            for p in range(NPAIR):
                step(NB - 1, p)

        def some(b):
            return not isinstance(b, int) or 0 <= b < NB

        def least(b, n):
            return b if not isinstance(b, int) else min(b, n)

        @block.sync
        def _(sp):
            sp.dma_start(cst[:], const).then_inc(in_a, 16)
            xv = x_in.rearrange("b (t p) d -> p (b t) d", p=P)
            xr = xres[:].rearrange("p (n d) -> p n d", d=D)
            for i in range(4):
                n = NT // 4
                sp.dma_start(xr[:, i * n:(i + 1) * n, :], xv[:, i * n:(i + 1) * n, :]).then_inc(in_x[i], 16)
                if i == 0:
                    sp.dma_start(wa[:], w_a).then_inc(in_a, 16)
                    sp.dma_start(woa[:], wo_a).then_inc(in_a, 16)
                    sp.dma_start(ba[:], b_a).then_inc(in_a, 16)
                    sp.dma_start(boa[:], bo_a).then_inc(in_a, 16)
            for dst, src in ((cent_s, cent), (gb, ln_gb), (w1s, w1), (w2s, w2), (b1r, b1), (b2r, b2)):
                sp.dma_start(dst[:], src).then_inc(in_f, 16)
            for dst, src in ((wb, w_b), (wob, wo_b)):
                sp.dma_start(dst[:], src).then_inc(in_b, 16)
            sp.wait_ge(zeroed, 1)
            sp.dma_start(xs_dram.rearrange("(n p) d -> p n d", p=P),
                         view(zero, 0, [[0, NSLOT], [1, D]])).then_inc(filled, 16)

            def slots(k):
                def load(s):
                    sp.dma_start(xs[s % AHEAD][:], xs_dram[s * P:(s + 1) * P, :]).then_inc(f_ld[s % AHEAD], 16)

                def turn(s, i, q):
                    m = k * NSLOT + s
                    if s + AHEAD < NSLOT:
                        sp.wait_ge(f_tx, m + 1)
                        load(s + AHEAD)
                    sp.wait_ge(f_ys, m + 1)
                    sp.dma_start(ys_dram[s * P:(s + 1) * P, :], ys[q][:]).then_inc(f_st[q], 16)

                sp.wait_ge(f_sent, (k + 1) * NT * 16)
                need(sp, f_tx, k * NSLOT)
                for s in range(AHEAD):
                    load(s)
                slot_turns(turn)

            slots(0)
            slots(1)
            ov = out.rearrange("b (t p) d -> p (b t) d", p=P)
            for i in range(4):
                n = NT // 4
                sp.wait_ge(f_x, 4 + i + 1)
                sp.dma_start(ov[:, i * n:(i + 1) * n, :], xr[:, i * n:(i + 1) * n, :]).then_inc(stored, 16)
            sp.wait_ge(stored, 4 * 16)

        @block.gpsimd
        def _(pool):
            nc.gpsimd.memset(kT[:, 0:P], 0.0)
            nc.gpsimd.memset(vT[:].rearrange("p (b l) -> p b l", b=NB)[:, :, 0:P], 0.0)
            nc.gpsimd.memset(mhalf[:], -0.5)
            nc.gpsimd.memset(zero[:], 0.0)
            nc.gpsimd.memset(ones_bf[:], 1.0)
            nc.gpsimd.memset(ones_row[:], 1.0).then_inc(zeroed, 1)

            def products(b):
                pool.wait_ge(a_qkv, b + 1)
                if not isinstance(b, int) or b > 0:
                    pool.wait_ge(a_s, b)
                for s, off, step in POOL_PAIRS:
                    last = nc.gpsimd.tensor_tensor(
                        view(prod, s * L, [[L, 2], [1, L]]), view(qT, 0, [[0, 2], [1, L]]),
                        view(kT, off, [[step, 2], [1, L]]), ALU.mult)
                last.then_inc(a_qkp, 1)

            own = Own(pool, own_sum, 3)

            def add_up(b):
                own.turn(b)
                pool.wait_ge(a_pv, b + 1)
                own.after(nc.gpsimd.tensor_tensor(sum4[:], pv[:, 0:4 * L], pv[:, 4 * L:8 * L], ALU.add))
                own.after(nc.gpsimd.tensor_tensor(sum2[:], sum4[:, 0:2 * L], sum4[:, 2 * L:4 * L], ALU.add))
                own.after(nc.gpsimd.tensor_tensor(sum1[:], sum2[:, 0:L], sum2[:, L:2 * L], ALU.add))
                if not isinstance(b, int) or b > 0:
                    pool.wait_ge(a_y, b)
                nc.gpsimd.tensor_tensor(oT[:], sum1[:], base[:], ALU.add).then_inc(a_sum, 1)

            pool.wait_ge(zeroed, 1)
            for i, (lo, hi) in enumerate(GROUPS_A):
                pool.wait_ge(a_ve, i + 1)
                nc.gpsimd.tensor_tensor(rstd[:, lo:hi], veps[:, lo:hi], mhalf[:, lo:hi], ALU.pow).then_inc(a_rs, 1)

            def turn(i):
                if some(i + 1):
                    products(i + 1)
                if some(i - 2):
                    add_up(i - 2)

            rolled(pool, 2, 3, turn)

            def power(given, n, eps, root, told):
                pool.wait_ge(given, n)
                nc.gpsimd.tensor_tensor(root[:], eps[:], mhalf[:], ALU.pow).then_inc(told, 1)

            def ffn(k):
                power(f_ve, 2 * k + 1, veps, rstd, f_rs)
                power(f_ve2, k + 1, veps2, rstd2, f_rs2)

                def residual(b):
                    n = k * NB + b
                    pool.wait_ge(f_u, n + 1)
                    xb = xres[:, bass.ds(b * L, L)]
                    nc.gpsimd.tensor_tensor(xb, xb, xn[:], ALU.add).then_inc(f_res, 1)

                with pool.Fori(0, NB) as b:
                    residual(b)
                pool.wait_ge(f_row, k + 1)
                pool.wait_ge(f_vh, (k + 1) * NB)
                pool.wait_ge(filled, 16)
                for i in range(AHEAD):
                    need(pool, f_ld[i], 16 * seen(k, i, AHEAD))
                for t in range(NT):
                    nc.gpsimd.indirect_dma_start(
                        out=xs_dram, out_offset=bass.IndirectOffsetOnAxis(ap=row[:, t:t + 1], axis=0),
                        in_=vhat[:, t * D:(t + 1) * D], in_offset=None).then_inc(f_sent, 16)
                for i in range(2):
                    pool.wait_ge(f_st[i], 16 * seen(k + 1, i, 2))
                pool.wait_ge(f_sent, (k + 1) * NT * 16)
                for t in range(NT):
                    nc.gpsimd.indirect_dma_start(
                        out=back[:, t * D:(t + 1) * D], out_offset=None, in_=ys_dram,
                        in_offset=bass.IndirectOffsetOnAxis(ap=row[:, t:t + 1], axis=0)).then_inc(f_back[t // 4], 16)

            ffn(0)
            power(f_ve, 2, veps, rstd, f_rs)
            ffn(1)

        @block.scalar
        def _(act):
            def turned(b):
                act.wait_ge(a_xT, b + 1)
                if not isinstance(b, int) or b > 0:
                    act.wait_ge(a_proj, 2 * b)
                nc.scalar.copy(xnT[:], bank[0][:, 0:L]).then_inc(a_xTs, 1)

            def projected(b):
                act.wait_ge(a_proj, 2 * b + 1)
                if not isinstance(b, int) or b > 0:
                    act.wait_ge(a_qk, b)
                    act.wait_ge(a_qkp, b)
                nc.scalar.activation(qT[:], bank[1][:, 0:L], ACT.Identity, bias=ba[:, 0:1])
                nc.scalar.activation(kT[:, P:P + L], bank[1][:, L:2 * L], ACT.Identity, bias=ba[:, 1:2])
                act.wait_ge(a_proj, 2 * b + 2)
                nc.scalar.activation(vT[:, bass.ds(b * (P + L) + P, L)], bank[0][:, L:2 * L], ACT.Identity,
                                     bias=ba[:, 2:3], accum_out=vsum[:, bass.ds(b, 1)]).then_inc(a_qkv, 1)

            def exps(b):
                act.wait_ge(a_sm, b + 1)
                nc.scalar.activation(ex[:], ex[:], ACT.Exp, scale=ISCALE_A).then_inc(a_e, 1)

            def widen(b):
                act.wait_ge(a_w, b + 1)
                if not isinstance(b, int) or b > 0:
                    act.wait_ge(a_wT, b)
                nc.scalar.copy(view(wide_w, 0, [[D, T * NS], [DHA, HA], [1, DHA]]),
                               view(wgt, 0, [[HA, T * NS], [1, HA], [0, DHA]])).then_inc(a_ww, 1)

            act.wait_ge(in_a, 5 * 16)
            act.wait_ge(zeroed, 1)

            def turn(i):
                if some(i):
                    exps(i)
                if some(i + 2):
                    turned(i + 2)
                    projected(i + 2)
                if some(i):
                    widen(i)

            rolled(act, 2, 3, turn)

            def ffn(k):
                def prepare(b):
                    n = k * NB + b
                    act.wait_ge(f_u, n + 1)
                    for t in range(T):
                        last = nc.scalar.mul(vhat[:, bass.ds((b * T + t) * D, D)], xn[:, t * D:(t + 1) * D],
                                             rstd2[:, bass.ds(b * T + t, 1)])
                    last.then_inc(f_vh, 1)
                    act.wait_ge(f_uT, n + 1)
                    need(act, f_aff, n)
                    nc.scalar.copy(xnT[:], bank[0][:, 0:L]).then_inc(f_uTs, 1)

                act.wait_ge(f_rs2, k + 1)
                prepare(0)
                with act.Fori(1, NB) as b:
                    prepare(b)
                act.wait_ge(f_am, k + 1)
                nc.scalar.activation(alpha[:], amax[:], ACT.Exp).then_inc(f_ea, 1)

                def copy_x(s, i, q):
                    m = k * NSLOT + s
                    act.wait_ge(f_tx, m + 1)
                    need(act, f_h, m - 1)
                    nc.scalar.copy(xsT[q][:], bank[0][:, 0:P]).then_inc(f_xs, 1)

                def turn(s, i, q):
                    m = k * NSLOT + s
                    act.wait_ge(f_th, m + 1)
                    need(act, f_y, m - 1)
                    nc.scalar.activation(hT[q][:], wide[:, q * 512:q * 512 + F], ACT.Relu).then_inc(f_hr, 1)
                    if s + 2 < NSLOT:
                        copy_x(s + 2, i + 1, q)

                copy_x(0, 0, 0)
                copy_x(1, 0, 1)
                slot_turns(turn)

            ffn(0)

            def exp_b(g):
                q = g_mod(g, 2)
                act.wait_ge(b_mx, g_(g) + 1)
                need(act, b_t, 2 * g_(g) - 2)
                for hh in range(2):
                    for t in range(T):
                        lo, hi = (0, P) if t == 0 else (P, BLOCKS * P)
                        last = nc.scalar.activation(
                            pb[:, q * 768 + hh * 384 + lo:q * 768 + hh * 384 + hi],
                            wide[:, q * 1024 + hh * 512 + lo:q * 1024 + hh * 512 + hi], ACT.Exp,
                            bias=nmax[:, q * 4 + t * 2 + hh:q * 4 + t * 2 + hh + 1],
                            accum_out=psum[:, q * 4 + t * 2 + hh:q * 4 + t * 2 + hh + 1])
                last.then_inc(b_e, 1)

            def copy_qk(n):
                r = g_mod(n, RING)
                act.wait_ge(b_j, g_(n) + 1)
                need(act, b_s, g_(n) - RING + 1)
                nc.scalar.copy(qk[:, r * 2 * L:(r + 1) * 2 * L], jb).then_inc(b_qk, 1)

            def copy_xT(b):
                act.wait_ge(b_xT, b + 1)
                nc.scalar.copy(xnT[:], jb[:, 0:L]).then_inc(b_xTs, 1)

            def step(b, p):
                g = (b, p)
                act.wait_ge(b_t, 2 * g_(g) + 1)
                need(act, b_pv, g_(g))
                nc.scalar.copy(pT[:, 0:384], bank[0][:, 0:384]).then_inc(b_ta, 1)
                if pair_ok(b, p + 1):
                    exp_b(at(b, p + 1))
                if pair_ok(b, p + 4):
                    copy_qk(at(b, p + 4))
                if p == 3 and pair_ok(b, p + 8):
                    copy_xT(b + 1)
                act.wait_ge(b_pv, g_(g) + 1)
                if p == 0:
                    need(act, b_o, b)
                nc.scalar.copy(zT[:, p * L:(p + 1) * L], bank[2][:, 0:L]).then_inc(b_zTs, 1)

            copy_xT(0)
            for n in range(RING):
                copy_qk((0, n))
            exp_b((0, 0))
            all_steps(act, step)
            ffn(1)

        @block.tensor
        def _(pe):
            def turn_xn(b):
                pe.wait_ge(a_xn, b + 1)
                if not isinstance(b, int) or b > 0:
                    pe.wait_ge(a_qkv, b)
                if not isinstance(b, int) or b > 4:
                    pe.wait_ge(a_x, b - 4)
                for t in range(T):
                    last = nc.tensor.transpose(bank[0][:, t * P:(t + 1) * P], xn[:, t * D:(t + 1) * D], ident)
                last.then_inc(a_xT, 1)

            def project(b):
                pe.wait_ge(a_xTs, b + 1)
                for i in range(3):
                    dst = bank[0][:, L:2 * L] if i == 2 else bank[1][:, i * L:(i + 1) * L]
                    mm = nc.tensor.matmul(dst, wa[:, i * D:(i + 1) * D], xnT[:], start=True, stop=True)
                    if i:
                        mm.then_inc(a_proj, 1)

            def score(b):
                pe.wait_ge(a_qk, b + 1)
                pe.wait_ge(a_qkp, b + 1)
                if not isinstance(b, int) or b > 0:
                    pe.wait_ge(a_sm, b)
                for t in range(T):
                    for s in range(ND):
                        last = nc.tensor.matmul(
                            bank[2][:, (t * ND + s) * HA:(t * ND + s + 1) * HA],
                            prod[:, s * L + t * P:s * L + (t + 1) * P], cst[:, C_HEAD:C_HEAD + HA],
                            start=True, stop=True)
                last.then_inc(a_s, 1)

            def turn_weights(b):
                pe.wait_ge(a_ww, b + 1)
                if not isinstance(b, int) or b > 0:
                    pe.wait_ge(a_pv, b)
                for s in range(NS):
                    for t in range(T):
                        last = nc.tensor.transpose(
                            wide[:, s * L + t * P:s * L + (t + 1) * P],
                            wide_w[:, (t * NS + s) * D:(t * NS + s + 1) * D], ident)
                last.then_inc(a_wT, 1)

            def out_proj(b):
                pe.wait_ge(a_sum, b + 1)
                need(pe, a_x, b)
                pe.wait_ge(a_qkv, least(b + 5, NB))
                for t in range(T):
                    dst = bank[0][:, t * P:(t + 1) * P]
                    nc.tensor.matmul(dst, oT[:, t * P:(t + 1) * P], woa[:], start=True, stop=False)
                    last = nc.tensor.matmul(dst, ones_row[:], boa[:], start=False, stop=True)
                last.then_inc(a_y, 1)

            pe.wait_ge(in_a, 5 * 16)
            pe.wait_ge(zeroed, 1)

            def turn(i):
                if some(i - 3):
                    out_proj(i - 3)
                if some(i + 2):
                    turn_xn(i + 2)
                if some(i - 1):
                    turn_weights(i - 1)
                if some(i + 2):
                    project(i + 2)
                if some(i + 1):
                    score(i + 1)

            rolled(pe, 2, 3, turn)

            def ffn(k):
                def prepare(b):
                    n = k * NB + b
                    pe.wait_ge(f_u, n + 1)
                    if k == 0 and isinstance(b, int):
                        pe.wait_ge(a_x, NB)
                    need(pe, f_uTs, n)
                    for t in range(T):
                        last = nc.tensor.transpose(bank[0][:, t * P:(t + 1) * P], xn[:, t * D:(t + 1) * D], ident)
                    last.then_inc(f_uT, 1)
                    pe.wait_ge(f_uTs, n + 1)
                    for t in range(T):
                        last = nc.tensor.matmul(bank[1][:, bass.ds((b * T + t) * NE, NE)],
                                                xnT[:, t * P:(t + 1) * P], cent_s[:], start=True, stop=True)
                    last.then_inc(f_aff, 1)

                if k == 0:
                    pe.wait_ge(in_r, 1)
                    pe.wait_ge(in_f, 6 * 16)
                prepare(0)
                with pe.Fori(1, NB) as b:
                    prepare(b)
                pe.wait_ge(f_oh, k + 1)
                nc.tensor.matmul(bank[2][:, 0:NT * NE], before[:], onehot[:], start=True, stop=False,
                                 skip_group_check=True)
                for t in range(NT):
                    last = nc.tensor.matmul(view(bank[2], (t + 1) * NE, [[NE, NT - t], [1, NE]]), ones_bf[:],
                                            view(onehot, t * NE, [[0, NT - t], [1, NE]]),
                                            start=False, stop=t == NT - 1, skip_group_check=True)
                last.then_inc(f_rank, 1)
                if k == 0:
                    for e in range(NE + 2):
                        if e > 1:
                            pe.wait_ge(f_biass, e - 1)
                        dst = wide[:, e % 2 * 512:(e % 2 + 1) * 512]
                        if e < NE:
                            nc.tensor.matmul(dst, view(gb, NE + e, [[0, P]]), w1s[:, e * F:(e + 1) * F],
                                             start=True, stop=False)
                            nc.tensor.matmul(dst, ones_row[:], b1r[:, e * F:(e + 1) * F], start=False,
                                             stop=True).then_inc(f_bias, 1)
                        else:
                            nc.tensor.matmul(dst, ones_row[:], b2r[:, (e - NE) * 512:(e - NE + 1) * 512],
                                             start=True, stop=True).then_inc(f_bias, 1)
                    pe.wait_ge(f_biass, NE + 2)
                    pe.wait_ge(f_w1, 1)

                def turn_x(s, i, q):
                    m = k * NSLOT + s
                    pe.wait_ge(f_ld[s % AHEAD], 16 * (seen(k, s, AHEAD) + 1))
                    need(pe, f_xs, m)
                    nc.tensor.transpose(bank[0][:, 0:P], xs[s % AHEAD][:], ident).then_inc(f_tx, 1)

                def hidden(s, i, q):
                    m = k * NSLOT + s
                    pe.wait_ge(f_xs, m + 1)
                    need(pe, f_hb, m - 1)
                    nc.tensor.matmul(bank[1 + q][:], xsT[q][:], w1s[:, bass.ds(at_e[s], F)], start=True,
                                     stop=True).then_inc(f_h, 1)

                def turn_h(s, i, q):
                    m = k * NSLOT + s
                    pe.wait_ge(f_hb, m + 1)
                    need(pe, f_hr, m - 1)
                    for c in range(FC):
                        last = nc.tensor.transpose(wide[:, q * 512 + c * P:q * 512 + (c + 1) * P],
                                                   hid[:, c * P:(c + 1) * P], ident)
                    last.then_inc(f_th, 1)

                def output(s, i, q):
                    m = k * NSLOT + s
                    pe.wait_ge(f_hr, m + 1)
                    need(pe, f_ys, m - 1)
                    for c in range(FC):
                        last = nc.tensor.matmul(wide[:, (2 + q) * 512:(2 + q) * 512 + D], hT[q][:, c * P:(c + 1) * P],
                                                w2s[:, bass.ds(at_e[s] + c * D, D)], start=c == 0,
                                                stop=c == FC - 1)
                    last.then_inc(f_y, 1)

                def turn(s, i, q):
                    turn_h(s, i, q)
                    if s + 1 < NSLOT:
                        hidden(s + 1, i + q, 1 - q)
                    if s + 2 < NSLOT:
                        turn_x(s + 2, i + 1, q)
                    output(s, i, q)

                pe.wait_ge(f_own, k + 1)
                at_e = experts(mybir.EngineType.PE)
                turn_x(0, 0, 0)
                hidden(0, 0, 0)
                turn_x(1, 0, 1)
                slot_turns(turn)

            ffn(0)

            def turn_xb(b):
                pe.wait_ge(b_xn, b + 1)
                for t in range(T):
                    last = nc.tensor.transpose(jb[:, t * P:(t + 1) * P], xn[:, t * D:(t + 1) * D], ident)
                last.then_inc(b_xT, 1)
                return b_xTs, b + 1

            def project_qk(g):
                for i in range(2):
                    c = i * HB * DHB + g[1] * P
                    last = nc.tensor.matmul(jb[:, i * L:(i + 1) * L], wb[:, c:c + P], xnT[:], start=True, stop=True)
                last.then_inc(b_j, 1)
                return b_qk, g_(g) + 1

            def project_v(b, i):
                c = 2 * HB * DHB + i // 2 * 512
                nc.tensor.matmul(jb, xnT[:, i % 2 * P:(i % 2 + 1) * P], wb[:, c:c + 512], start=True,
                                 stop=True).then_inc(b_vp, 1)
                return b_v, 4 * b + i + 1

            def out_proj_b(b):
                pe.wait_ge(b_zTs, NPAIR * (b + 1))
                for t in range(T):
                    for p in range(NPAIR):
                        last = nc.tensor.matmul(jb[:, t * P:(t + 1) * P], zT[:, p * L + t * P:p * L + (t + 1) * P],
                                                wob[:, p * D:(p + 1) * D], start=p == 0, stop=p == NPAIR - 1)
                last.then_inc(b_o, 1)
                return b_x, b + 1

            def scores_b(g):
                q, r = g_mod(g, 2), g_mod(g, RING)
                pe.wait_ge(b_qk, g_(g) + 1)
                need(pe, b_e, g_(g) - 1)
                for hh in range(2):
                    nc.tensor.matmul(view(wide, q * 1024 + hh * 512, [[2 * P, 2], [1, P]]), id_bf[:],
                                     view(causal, 0, [[0, 2], [1, P]]), start=True, stop=False,
                                     skip_group_check=True)
                for t in range(T):
                    for hh in range(2):
                        rows = slice(hh * DHB, (hh + 1) * DHB)
                        lo, hi = (0, P) if t == 0 else (P, BLOCKS * P)
                        last = nc.tensor.matmul(
                            wide[:, q * 1024 + hh * 512 + lo:q * 1024 + hh * 512 + hi],
                            qk[rows, r * 2 * L + t * P:r * 2 * L + (t + 1) * P],
                            qk[rows, r * 2 * L + L:r * 2 * L + L + hi - lo],
                            start=False, stop=t == T - 1, skip_group_check=True)
                last.then_inc(b_s, 1)

            def turn_p(g):
                q = g_mod(g, 2)
                pe.wait_ge(b_n, g_(g) + 1)
                for hh, free in ((0, b_ta), (1, b_tb)):
                    need(pe, free, g_(g))
                    for c in range(BLOCKS):
                        o = q * 768 + hh * 384 + c * P
                        last = nc.tensor.transpose(bank[hh][:, c * P:(c + 1) * P], pb[:, o:o + P], ident)
                    last.then_inc(b_t, 1)

            def values_b(g):
                need(pe, b_zTs, g_(g))
                if g[1] % 4 == 0:
                    pe.wait_ge(b_v, 4 * g[0] + g[1] // 4 * 2 + 2)
                pe.wait_ge(b_ta, g_(g) + 1)
                pe.wait_ge(b_tb, g_(g) + 1)
                for kt in range(T):
                    for hh in range(2):
                        c = hh * 384 + kt * 2 * P
                        v = (kt * HB + 2 * g[1] + hh) * DHB
                        last = nc.tensor.matmul(bank[2][hh * DHB:(hh + 1) * DHB, kt * P:L], vb[:, v:v + DHB],
                                                pT[:, c:c + L - kt * P], start=kt == 0, stop=kt == T - 1,
                                                skip_group_check=True)
                last.then_inc(b_pv, 1)

            def step(b, p):
                g = (b, p)
                free = {0: (b_qk, g_(g) + RING), 1: (b_x, b), 2: (b_v, 4 * b + 3), 3: (b_v, 4 * b + 4),
                        4: (b_xTs, b + 2), 5: (b_v, 4 * b + 5), 6: (b_v, 4 * b + 6), 7: (b_qk, g_(g) + RING)}[p]
                if isinstance(b, int) and b == 0 and p == 1:
                    free = b_qk, g_(g) + RING
                turn_p(g)
                if pair_ok(b, p + 2):
                    scores_b(at(b, p + 2))
                if pair_ok(b, p + RING):
                    need(pe, *free)
                    free = project_qk(at(b, p + RING))
                values_b(g)
                if p == 0 and (not isinstance(b, int) or b > 0):
                    need(pe, *free)
                    out_proj_b(b - 1)
                if p in (1, 2):
                    need(pe, *free)
                    project_v(b, p + 1)
                if p == 3 and pair_ok(b, p + NPAIR):
                    need(pe, *free)
                    turn_xb(b + 1)
                if p in (4, 5) and pair_ok(b, p + NPAIR):
                    need(pe, *free)
                    project_v(b + 1, p - 4)

            need(pe, f_ys, NSLOT)
            pe.wait_ge(b_w, 1)
            free = turn_xb(0)
            for i in range(2):
                need(pe, *free)
                free = project_v(0, i)
            for n in range(RING):
                need(pe, *free)
                free = project_qk((0, n))
            scores_b((0, 0))
            scores_b((0, 1))
            all_steps(pe, step)
            need(pe, b_x, NB - 1)
            out_proj_b(NB - 1)
            ffn(1)

        @block.vector
        def _(dve):
            def xtile(b, t):
                return xres[:, bass.ds((b * T + t) * D, D)]

            def statistics(lo, hi, done):
                for t in range(lo, hi):
                    last = nc.vector.bn_stats(stat[:, t * 6:(t + 1) * 6], xres[:, t * D:(t + 1) * D])
                lno.after(last)
                for t in range(lo, hi):
                    last = nc.vector.bn_aggr(mv[:, t * 2:(t + 1) * 2], stat[:, t * 6:(t + 1) * 6])
                lno.after(last)
                nc.vector.tensor_scalar(veps[:, lo:hi], view(mv, 2 * lo + 1, [[2, hi - lo]]), EPS, None,
                                        ALU.add).then_inc(done, 1)

            lno = Own(dve, own_ln, 100)
            lno.turn(0)

            def norm(b, read, done):
                if not isinstance(b, int) or b > 0:
                    dve.wait_ge(read, b)
                for t in range(T):
                    last = nc.vector.tensor_scalar(xn[:, t * D:(t + 1) * D], xtile(b, t),
                                                   mv[:, bass.ds((b * T + t) * 2, 1)],
                                                   rstd[:, bass.ds(b * T + t, 1)], ALU.subtract, ALU.mult)
                last.then_inc(done, 1)

            def norm_a(b):
                norm(b, a_xT, a_xn)

            def products(b):
                dve.wait_ge(a_qkv, b + 1)
                if not isinstance(b, int) or b > 0:
                    dve.wait_ge(a_s, b)
                for s, off, step in DVE_PAIRS:
                    nc.vector.tensor_tensor(view(prod, s * L, [[L, 2], [1, L]]), view(qT, 0, [[0, 2], [1, L]]),
                                            view(kT, off, [[step, 2], [1, L]]), ALU.mult)
                nc.vector.tensor_tensor(prod[:, (ND - 1) * L:ND * L], qT[:], kT[:, P:P + L],
                                        ALU.mult).then_inc(a_qk, 1)

            smo = Own(dve, own_sm, 2)

            def less_max(b):
                smo.turn(b)
                dve.wait_ge(a_s, b + 1)
                smo.after(nc.vector.tensor_reduce(smax[:].rearrange("p (t h) -> p t h", t=T),
                                                  view(bank[2], 0, [[ND * HA, T], [1, HA], [HA, ND]]),
                                                  AX.X, ALU.max))
                smo.after(nc.vector.tensor_scalar(smax[:], smax[:], 0.0, None, ALU.max))
                for t in range(T):
                    nc.vector.tensor_tensor(view(ex, t * NS * HA, [[HA, ND], [1, HA]]),
                                            view(bank[2], t * ND * HA, [[HA, ND], [1, HA]]),
                                            view(smax, t * HA, [[0, ND], [1, HA]]), ALU.subtract)
                nc.vector.tensor_scalar(view(ex, ND * HA, [[NS * HA, T], [1, HA]]),
                                        smax[:].rearrange("p (t h) -> p t h", t=T), -1.0, None,
                                        ALU.mult).then_inc(a_sm, 1)

            wo = Own(dve, own_w, 4)

            def weights(b):
                wo.turn(b)
                dve.wait_ge(a_e, b + 1)
                e9 = view(ex, ND * HA, [[NS * HA, T], [1, HA]])
                if not isinstance(b, int) or b > 0:
                    dve.wait_ge(a_ww, b)
                for t in range(T):
                    last = nc.vector.tensor_tensor(view(wgt, t * NS * HA, [[HA, ND], [1, HA]]),
                                                   view(ex, t * NS * HA, [[HA, ND], [1, HA]]),
                                                   view(ex, (t * NS + ND) * HA, [[0, ND], [1, HA]]), ALU.subtract)
                wo.after(last)
                wo.after(nc.vector.tensor_reduce(zsum[:].rearrange("p (t h) -> p t h", t=T),
                                                 view(wgt, 0, [[NS * HA, T], [1, HA], [HA, ND]]), AX.X, ALU.add))
                wo.after(nc.vector.scalar_tensor_tensor(zall[:].rearrange("p (t h) -> p t h", t=T), e9, float(L),
                                                        zsum[:].rearrange("p (t h) -> p t h", t=T),
                                                        ALU.mult, ALU.add))
                wo.after(nc.vector.reciprocal(zinv[:], zall[:]))
                for t in range(T):
                    w9 = view(wgt, t * NS * HA, [[HA, ND], [1, HA]])
                    nc.vector.tensor_tensor(w9, w9, view(zinv, t * HA, [[0, ND], [1, HA]]), ALU.mult)
                nc.vector.tensor_tensor(view(wgt, ND * HA, [[NS * HA, T], [1, HA]]), e9,
                                        zinv[:].rearrange("p (t h) -> p t h", t=T), ALU.mult).then_inc(a_w, 1)

            pvo = Own(dve, own_pv, 1)

            def weigh_values(b):
                pvo.turn(b)
                dve.wait_ge(a_wT, b + 1)
                if not isinstance(b, int) or b > 0:
                    dve.wait_ge(a_sum, b)
                for s, off, step in PAIRS:
                    v = bass.AP(vT, b * (P + L) + off, [[NB * (P + L), P], [step, 2], [1, L]])
                    nc.vector.tensor_tensor(view(pv, s * L, [[L, 2], [1, L]]),
                                            view(wide, s * L, [[L, 2], [1, L]]), v, ALU.mult)
                s = ND - 1
                pvo.after(nc.vector.tensor_tensor(pv[:, s * L:(s + 1) * L], wide[:, s * L:(s + 1) * L],
                                                  vT[:, bass.ds(b * (P + L) + P, L)], ALU.mult))
                nc.vector.scalar_tensor_tensor(base[:], wide[:, ND * L:NS * L], vsum[:, bass.ds(b, 1)],
                                               pv[:, s * L:(s + 1) * L], ALU.mult, ALU.add).then_inc(a_pv, 1)

            def residual_a(b):
                dve.wait_ge(a_y, b + 1)
                xb = xres[:, bass.ds(b * L, L)]
                nc.vector.tensor_tensor(xb, xb, bank[0][:, 0:L], ALU.add).then_inc(a_x, 1)

            dve.wait_ge(in_a, 5 * 16)
            nc.vector.tensor_copy(before[:], cst[:, C_BEFORE:C_BEFORE + P])
            nc.vector.tensor_copy(id_bf[:], ident)
            nc.vector.tensor_copy(causal[:], cst[:, C_CAUSAL:C_CAUSAL + P]).then_inc(in_r, 1)
            done = 0
            for i, (lo, hi) in enumerate(GROUPS_A):
                while done < hi:
                    dve.wait_ge(in_x[done // 4], 16)
                    done += 4
                statistics(lo, hi, a_ve)
            dve.wait_ge(a_rs, len(GROUPS_A))

            def turn(i):
                if some(i):
                    less_max(i)
                if some(i + 1):
                    products(i + 1)
                if some(i + 2):
                    norm_a(i + 2)
                if some(i):
                    weights(i)
                if some(i - 3):
                    residual_a(i - 3)
                if some(i - 1):
                    weigh_values(i - 1)

            rolled(dve, 2, 3, turn)

            fo = Own(dve, own_f, 1000)
            fo.turn(0)

            def experts_of(v):
                return v[:].rearrange("p (t e) -> p t e", e=NE)

            def ffn(k):
                if k == 0:
                    dve.wait_ge(a_x, NB)
                    statistics(0, NT, f_ve)
                dve.wait_ge(f_rs, 2 * k + 1)
                var = view(mv, 1, [[2, NT]])
                fo.after(nc.vector.tensor_tensor(var2[:], var, rstd[:], ALU.mult))
                fo.after(nc.vector.tensor_tensor(var2[:], var2[:], rstd[:], ALU.mult))
                nc.vector.tensor_scalar(veps2[:], var2[:], EPS, None, ALU.add).then_inc(f_ve2, 1)

                def normed(b):
                    n = k * NB + b
                    need(dve, f_uT, n)
                    need(dve, f_vh, n)
                    need(dve, f_res, n)
                    for t in range(T):
                        last = nc.vector.tensor_scalar(xn[:, t * D:(t + 1) * D], xtile(b, t),
                                                       mv[:, bass.ds((b * T + t) * 2, 1)],
                                                       rstd[:, bass.ds(b * T + t, 1)], ALU.subtract, ALU.mult)
                    last.then_inc(f_u, 1)

                normed(0)
                with dve.Fori(1, NB) as b:
                    normed(b)

                dve.wait_ge(f_aff, (k + 1) * NB)
                aff = bank[1][:, 0:NT * NE].rearrange("p (t e) -> p t e", e=NE)
                fo.after(nc.vector.tensor_reduce(amax[:], aff, AX.X, ALU.max))
                fo.after(nc.vector.tensor_tensor(experts_of(pick), aff, view(amax, 0, [[1, NT], [0, NE]]), ALU.is_equal))
                fo.after(nc.vector.tensor_tensor(experts_of(pick2), experts_of(pick),
                                                 view(cst, C_FIRST, [[0, NT], [1, NE]]), ALU.mult))
                fo.after(nc.vector.tensor_reduce(pmax[:], experts_of(pick2), AX.X, ALU.max))
                nc.vector.tensor_tensor(experts_of(onehot), experts_of(pick2), view(pmax, 0, [[1, NT], [0, NE]]),
                                        ALU.is_equal).then_inc(f_oh, 1)
                nc.vector.tensor_scalar(amax[:], amax[:], -1.0, 80.0, ALU.mult, ALU.min).then_inc(f_am, 1)

                dve.wait_ge(f_rank, k + 1)
                total = bank[2][:, NT * NE:(NT + 1) * NE]
                fo.after(nc.vector.tensor_scalar(tiles[:], total, 1.0 / P, 0.5 - 1.0 / (2 * P), ALU.mult, ALU.add))
                fo.after(nc.vector.tensor_scalar(tiles_r[:], tiles[:], 8388608.0, None, ALU.add))
                fo.after(nc.vector.tensor_scalar(tiles[:], tiles_r[:], 8388608.0, None, ALU.subtract))
                up = upto[:].rearrange("p (a b) -> p a b", b=NE)
                fo.after(nc.vector.tensor_tensor(up, view(cst, C_UPTO, [[NE, NE], [1, NE]]),
                                                 view(tiles, 0, [[0, NE], [1, NE]]), ALU.mult))
                fo.after(nc.vector.tensor_reduce(end[:], up, AX.X, ALU.add))
                fo.after(nc.vector.tensor_tensor(start[:], end[:], tiles[:], ALU.subtract))
                fo.after(nc.vector.tensor_scalar(start_r[:], start[:], float(P), None, ALU.mult))
                fo.after(nc.vector.tensor_tensor(experts_of(pick), bank[2][:, 0:NT * NE].rearrange(
                    "p (t e) -> p t e", e=NE), view(start_r, 0, [[0, NT], [1, NE]]), ALU.add))
                fo.after(nc.vector.tensor_tensor(pick2[:], pick[:], onehot[:], ALU.mult))
                fo.after(nc.vector.tensor_reduce(row_f[:], experts_of(pick2), AX.X, ALU.add))
                nc.vector.tensor_copy(row[:], row_f[:]).then_inc(f_row, 1)
                fo.after(nc.vector.tensor_tensor(past[:].rearrange("p (s e) -> p s e", e=NE),
                                                 view(end, 0, [[0, NSLOT], [1, NE]]),
                                                 view(cst, C_SLOT, [[1, NSLOT], [0, NE]]), ALU.is_le))
                fo.after(nc.vector.tensor_reduce(owner_f[:], past[:].rearrange("p (s e) -> p s e", e=NE),
                                                 AX.X, ALU.add))
                nc.vector.tensor_scalar(owner[:], owner_f[:], float(NE - 1), float(F), ALU.min,
                                        ALU.mult).then_inc(f_own, 1)
                dve.wait_ge(f_ea, k + 1)
                fo.after(nc.vector.tensor_scalar(pmax[:], alpha[:], 1.0, None, ALU.add))
                fo.after(nc.vector.reciprocal(alpha[:], pmax[:]))
                if k == 0:
                    for e in range(NE + 2):
                        dve.wait_ge(f_bias, e + 1)
                        dst = bias1[:, e * F:(e + 1) * F] if e < NE else bias2[:, (e - NE) * 512:(e - NE + 1) * 512]
                        nc.vector.tensor_copy(dst, wide[:, e % 2 * 512:(e % 2 + 1) * 512]).then_inc(f_biass, 1)
                    for e in range(NE):
                        last = nc.vector.tensor_scalar(w1s[:, e * F:(e + 1) * F], w1s[:, e * F:(e + 1) * F],
                                                       gb[:, e:e + 1], None, ALU.mult)
                    last.then_inc(f_w1, 1)

                def add_bias(s, i, q):
                    m = k * NSLOT + s
                    dve.wait_ge(f_h, m + 1)
                    need(dve, f_th, m)
                    nc.vector.tensor_tensor(hid[:], bank[1 + q][:], bias1[:, bass.ds(at_e[s], F)],
                                            ALU.add).then_inc(f_hb, 1)

                def turn(s, i, q):
                    m = k * NSLOT + s
                    if s + 1 < NSLOT:
                        add_bias(s + 1, i + q, 1 - q)
                    dve.wait_ge(f_y, m + 1)
                    need(dve, f_st[q], 16 * seen(k, s, 2))
                    nc.vector.tensor_tensor(ys[q][:], wide[:, (2 + q) * 512:(2 + q) * 512 + D],
                                            bias2[:, bass.ds(at_e[s] // FC, D)], ALU.add).then_inc(f_ys, 1)

                dve.wait_ge(f_own, k + 1)
                at_e = experts(mybir.EngineType.DVE)
                add_bias(0, 0, 0)
                slot_turns(turn)

                for i in range(4):
                    dve.wait_ge(f_back[i], (k + 1) * 4 * 16)
                    if i == 0:
                        dve.wait_ge(f_res, (k + 1) * NB)
                    for t in range(4 * i, 4 * i + 4):
                        xt = xres[:, t * D:(t + 1) * D]
                        last = nc.vector.scalar_tensor_tensor(xt, back[:, t * D:(t + 1) * D], alpha[:, t:t + 1], xt,
                                                              ALU.mult, ALU.add)
                    last.then_inc(f_x, 1)

            ffn(0)
            dve.wait_ge(f_x, 4)
            statistics(0, NT, f_ve)
            dve.wait_ge(f_rs, 2)

            def norm_b(b):
                need(dve, b_xT, b)
                for t in range(T):
                    last = nc.vector.tensor_scalar(xn[:, t * D:(t + 1) * D], xtile(b, t),
                                                   mv[:, bass.ds((b * T + t) * 2, 1)],
                                                   rstd[:, bass.ds(b * T + t, 1)], ALU.subtract, ALU.mult)
                last.then_inc(b_xn, 1)

            def copy_v(b, i):
                dve.wait_ge(b_vp, 4 * b + i + 1)
                need(dve, b_pv, NPAIR * b - 4 if i < 2 else NPAIR * b)
                c = (i % 2 * HB + i // 2 * 8) * DHB
                nc.vector.tensor_copy(vb[:, c:c + 8 * DHB], jb).then_inc(b_v, 1)

            def max_b(g):
                q = g_mod(g, 2)
                dve.wait_ge(b_s, g_(g) + 1)
                for t in range(T):
                    last = nc.vector.tensor_reduce(
                        nmax[:, q * 4 + t * 2:q * 4 + t * 2 + 2],
                        view(wide, q * 1024 + t * P, [[512, 2], [1, (t + 1) * P]]), AX.X, ALU.max, negate=True)
                last.then_inc(b_mx, 1)

            no = Own(dve, own_n, 1)

            def divide(g):
                q = g_mod(g, 2)
                no.turn(g_(g))
                dve.wait_ge(b_e, g_(g) + 1)
                no.after(nc.vector.reciprocal(prec[:], psum[:, q * 4:q * 4 + 4]))
                for hh in range(2):
                    for t in range(T):
                        o = q * 768 + hh * 384 + t * P
                        px = pb[:, o:o + (t + 1) * P]
                        last = nc.vector.tensor_scalar(px, px, prec[:, t * 2 + hh:t * 2 + hh + 1], None, ALU.mult)
                last.then_inc(b_n, 1)

            def residual_b(b):
                dve.wait_ge(b_o, b + 1)
                xb = xres[:, bass.ds(b * L, L)]
                nc.vector.tensor_tensor(xb, xb, jb[:, 0:L], ALU.add).then_inc(b_x, 1)

            def step(b, p):
                g = (b, p)
                dve.wait_ge(b_t, 2 * g_(g) + 2)
                need(dve, b_pv, g_(g))
                nc.vector.tensor_copy(pT[:, 384:768], bank[1][:, 0:384]).then_inc(b_tb, 1)
                if pair_ok(b, p + 1):
                    divide(at(b, p + 1))
                if pair_ok(b, p + 2):
                    max_b(at(b, p + 2))
                if p == 1 and pair_ok(b, p + NPAIR):
                    norm_b(b + 1)
                if p == 0 and (not isinstance(b, int) or b > 0):
                    residual_b(b - 1)
                if p in (1, 2):
                    copy_v(b, p + 1)
                if p in (4, 5) and pair_ok(b, p + NPAIR):
                    copy_v(b + 1, p - 4)

            dve.wait_ge(in_b, 2 * 16)
            nc.vector.tensor_scalar(wb[:, 0:HB * DHB], wb[:, 0:HB * DHB], float(DHB) ** -0.5, None,
                                    ALU.mult).then_inc(b_w, 1)
            norm_b(0)
            for i in range(2):
                copy_v(0, i)
            max_b((0, 0))
            max_b((0, 1))
            divide((0, 0))
            all_steps(dve, step)
            residual_b(NB - 1)
            dve.wait_ge(b_x, NB)
            statistics(0, NT, f_ve)
            ffn(1)


def kernel(**inputs):
    import numpy as np
    import concourse.bacc as bacc
    from concourse.bass_utils import run_bass_kernel_spmd as run

    a = {k.replace("L0_", ""): np.asarray(v) for k, v in inputs.items()}
    laid = {
        "x": a["attn_a_x"],
        "w_a": np.concatenate([a["attn_a_W" + i].T for i in "qkv"], axis=1),
        "wo_a": a["attn_a_Wo"].T,
        "b_a": np.stack([a["attn_a_b" + i] for i in "qkv"], axis=1),
        "bo_a": a["attn_a_bo"][None],
        "w_b": np.concatenate([a["attn_b_W_" + i].reshape(HB * DHB, D).T for i in "QKV"], axis=1),
        "wo_b": a["attn_b_W_O"].T.reshape(NPAIR, P, D).transpose(1, 0, 2).reshape(P, NPAIR * D),
        "cent": a["ffn_centroids"].T,
        "ln_gb": np.concatenate([a["ffn_ln_g"].T, a["ffn_ln_b"].T], axis=1),
        "w1": a["ffn_w1"].transpose(2, 0, 1).reshape(D, NE * F),
        "b1": a["ffn_b1"].reshape(1, NE * F),
        "w2": a["ffn_w2"].reshape(NE, D, FC, P).transpose(3, 0, 2, 1).reshape(P, NE * FC * D),
        "b2": a["ffn_b2"].reshape(1, NE * D),
        "const": constants(),
    }
    nc = bacc.Bacc("TRN2", target_bir_lowering=False, num_devices=1)
    arrays, args = {}, []
    for name, v in laid.items():
        v = np.ascontiguousarray(v)
        arrays["in_" + name] = v
        args.append(nc.dram_tensor("in_" + name, v.shape, mybir.dt.from_np(v.dtype), kind="ExternalInput").ap())
    args.append(nc.dram_tensor("out_0", (NB, L, D), F32, kind="ExternalOutput").ap())
    hybrid_layer(nc, *args)
    return run(nc, [arrays], core_ids=[0]).results[0]["out_0"]
```
